# Optimizing a Trainium2 kernel written in Bass

```python
import numpy as np
import jax
import jax.numpy as jnp

def _softmax(x, axis=-1):
    return jax.nn.softmax(x, axis=axis)

def _gelu(x):
    return jax.nn.gelu(x, approximate=True)

def _silu(x):
    return jax.nn.silu(x)

def _sigmoid(x):
    return jax.nn.sigmoid(x)

def _layernorm(x, axis=-1, eps=1e-05):
    m = jnp.mean(x, axis=axis, keepdims=True)
    v = jnp.var(x, axis=axis, keepdims=True)
    return (x - m) / jnp.sqrt(v + eps)

def _scatter_add(tgt, idx, src, axis=0):
    return tgt.at[idx].add(src)

def _segment_sum(src, seg, n):
    return jax.ops.segment_sum(src, seg, n)
kernel_name = 'mk_flamingo_gated_d1_seqx_r4_4a05f3'

def setup_inputs(seed: int=0):
    np.random.seed(seed)
    _w = jnp.asarray

    def _rec_inputs():
        import jax
        import jax.numpy as jnp
        _rk = jax.random.key(seed)
        x = -0.0002928 + 1 * jax.random.normal(jax.random.fold_in(_rk, 1), (16, 100, 256), jnp.float32)
        _lenS = 100 - jax.random.randint(jax.random.fold_in(_rk, 7), (16,), 0, max(1, 100 // 4) + 1, jnp.int32)
        _lenS2 = 361 - jax.random.randint(jax.random.fold_in(_rk, 8), (16,), 0, max(1, 361 // 4) + 1, jnp.int32)
        _ctx_1024P = jax.random.normal(jax.random.fold_in(_rk, 11), (16, 16, 256), jnp.float32)
        _ctx_1024c = jax.random.dirichlet(jax.random.fold_in(_rk, 511), 0.3 * jnp.ones((16,), jnp.float32), (16, 361))
        _ctx_1024t = jnp.einsum('bsk,bkd->bsd', _ctx_1024c, _ctx_1024P)
        _ctx_1024t = _ctx_1024t * jax.lax.rsqrt(jnp.mean(jnp.square(_ctx_1024t)) + 1e-12) * 0.953939
        ctx_1024 = -1.39393e-06 + 0.999914 * (_ctx_1024t + 0.3 * jax.random.normal(jax.random.fold_in(_rk, 611), (16, 361, 256), jnp.float32))
        _g = jax.random.normal(jax.random.fold_in(_rk, 9001), (2, 1), jnp.float32)
        _g = jnp.sign(_g) * jnp.maximum(jnp.abs(_g), 1.0) + (_g == 0) * 1.0
        g_xattn = _g[0]
        g_ffn = _g[1]
        return (x, ctx_1024, g_xattn, g_ffn)
    x, ctx_1024, g_xattn, g_ffn = _rec_inputs()

    def _L0_xattn_setup():
        import jax, jax.numpy as jnp
        import numpy as np
        D_MODEL = 256
        N_HEADS = 16
        D_HEAD = D_MODEL // N_HEADS
        key = jax.random.key(seed)
        ks = jax.random.split(key, 11)
        B, T = (2, 512)
        s = 1.0 / np.sqrt(D_MODEL)
        return {'query': jax.random.normal(ks[0], (B, T, D_MODEL), dtype=jnp.float32), 'key': jax.random.normal(ks[1], (B, T, D_MODEL), dtype=jnp.float32), 'value': jax.random.normal(ks[2], (B, T, D_MODEL), dtype=jnp.float32), 'Wq': jax.random.normal(ks[3], (D_MODEL, D_MODEL), dtype=jnp.float32) * s, 'bq': jnp.zeros((D_MODEL,), dtype=jnp.float32), 'Wk': jax.random.normal(ks[4], (D_MODEL, D_MODEL), dtype=jnp.float32) * s, 'bk': jnp.zeros((D_MODEL,), dtype=jnp.float32), 'Wv': jax.random.normal(ks[5], (D_MODEL, D_MODEL), dtype=jnp.float32) * s, 'bv': jnp.zeros((D_MODEL,), dtype=jnp.float32), 'Wh': jax.random.normal(ks[6], (D_MODEL, D_MODEL), dtype=jnp.float32) * s, 'bh': jnp.zeros((D_MODEL,), dtype=jnp.float32)}
    _L0_xattn_all = _L0_xattn_setup()
    _L0_xattn_in = {k: v for k, v in _L0_xattn_all.items() if k in ('Wq', 'bq', 'Wk', 'bk', 'Wv', 'bv', 'Wh', 'bh')}
    del _L0_xattn_all

    def _L0_ffn_setup():
        import jax, jax.numpy as jnp
        import numpy as np
        B, S, D, F, E, R, K = (1, 128, 256, 1024, 8, 16, 2)
        SCALING = 32.0 / 16.0
        EPS = 1e-06

        def _forward(x, norm_w, w1, w3, w2, gate_w, a1, b1, a3, b3, a2, b2):
            Bq, Sq, Dq = x.shape
            nx = x * jax.lax.rsqrt(jnp.mean(x * x, axis=-1, keepdims=True) + EPS) * norm_w
            t = nx.reshape(-1, Dq)
            probs = jax.nn.softmax(t @ gate_w.T, axis=-1)
            topw, topi = jax.lax.top_k(probs, K)
            topw = topw / jnp.sum(topw, axis=-1, keepdims=True)
            weights = jnp.sum(jax.nn.one_hot(topi, E, dtype=t.dtype) * topw[..., None], axis=1)
            base1 = t @ w1.T
            base3 = t @ w3.T
            h1 = base1[None] + SCALING * jnp.einsum('etr,efr->etf', jnp.einsum('td,erd->etr', t, a1), b1)
            h3 = base3[None] + SCALING * jnp.einsum('etr,efr->etf', jnp.einsum('td,erd->etr', t, a3), b3)
            act = jax.nn.silu(h1) * h3
            out_e = jnp.einsum('etf,df->etd', act, w2) + SCALING * jnp.einsum('etr,edr->etd', jnp.einsum('etf,erf->etr', act, a2), b2)
            out = jnp.einsum('te,etd->td', weights, out_e)
            return out.reshape(Bq, Sq, Dq)
        key = jax.random.key(seed)
        ks = jax.random.split(key, 12)
        w = lambda k, shape: jax.random.normal(k, shape, dtype=jnp.float32) * 0.02
        return {'x': jax.random.normal(ks[0], (B, S, D), dtype=jnp.float32), 'norm_w': jnp.ones((D,), jnp.float32), 'w1': w(ks[1], (F, D)), 'w3': w(ks[2], (F, D)), 'w2': w(ks[3], (D, F)), 'gate_w': w(ks[4], (E, D)), 'a1': w(ks[5], (E, R, D)), 'b1': w(ks[6], (E, F, R)), 'a3': w(ks[7], (E, R, D)), 'b3': w(ks[8], (E, F, R)), 'a2': w(ks[9], (E, R, F)), 'b2': w(ks[10], (E, D, R))}
    _L0_ffn_all = _L0_ffn_setup()
    _L0_ffn_in = {k: v for k, v in _L0_ffn_all.items() if k in ('norm_w', 'w1', 'w3', 'w2', 'gate_w', 'a1', 'b1', 'a3', 'b3', 'a2', 'b2')}
    del _L0_ffn_all
    return {'x': x, 'ctx_1024': ctx_1024, 'g_xattn': g_xattn, 'g_ffn': g_ffn, 'L0_xattn_Wq': _L0_xattn_in['Wq'], 'L0_xattn_bq': _L0_xattn_in['bq'], 'L0_xattn_Wk': _L0_xattn_in['Wk'], 'L0_xattn_bk': _L0_xattn_in['bk'], 'L0_xattn_Wv': _L0_xattn_in['Wv'], 'L0_xattn_bv': _L0_xattn_in['bv'], 'L0_xattn_Wh': _L0_xattn_in['Wh'], 'L0_xattn_bh': _L0_xattn_in['bh'], 'L0_ffn_norm_w': _L0_ffn_in['norm_w'], 'L0_ffn_w1': _L0_ffn_in['w1'], 'L0_ffn_w3': _L0_ffn_in['w3'], 'L0_ffn_w2': _L0_ffn_in['w2'], 'L0_ffn_gate_w': _L0_ffn_in['gate_w'], 'L0_ffn_a1': _L0_ffn_in['a1'], 'L0_ffn_b1': _L0_ffn_in['b1'], 'L0_ffn_a3': _L0_ffn_in['a3'], 'L0_ffn_b3': _L0_ffn_in['b3'], 'L0_ffn_a2': _L0_ffn_in['a2'], 'L0_ffn_b2': _L0_ffn_in['b2']}

def reference(x, ctx_1024, g_xattn, g_ffn, L0_xattn_Wq, L0_xattn_bq, L0_xattn_Wk, L0_xattn_bk, L0_xattn_Wv, L0_xattn_bv, L0_xattn_Wh, L0_xattn_bh, L0_ffn_norm_w, L0_ffn_w1, L0_ffn_w3, L0_ffn_w2, L0_ffn_gate_w, L0_ffn_a1, L0_ffn_b1, L0_ffn_a3, L0_ffn_b3, L0_ffn_a2, L0_ffn_b2):
    import jax
    import jax.numpy as jnp

    def _L0_xattn_ref(query, key, value, Wq, bq, Wk, bk, Wv, bv, Wh, bh):
        import jax, jax.numpy as jnp
        import numpy as np
        D_MODEL = 256
        N_HEADS = 16
        D_HEAD = D_MODEL // N_HEADS
        B, T_src, _ = query.shape
        T_dst = key.shape[1]
        Q = query @ Wq.T + bq
        K = key @ Wk.T + bk
        V = value @ Wv.T + bv
        Q = Q.reshape(B, T_src, N_HEADS, D_HEAD).transpose(0, 2, 1, 3)
        K = K.reshape(B, T_dst, N_HEADS, D_HEAD).transpose(0, 2, 1, 3)
        V = V.reshape(B, T_dst, N_HEADS, D_HEAD).transpose(0, 2, 1, 3)
        dot = jnp.einsum('bhsd,bhtd->bhst', Q, K) / np.sqrt(D_HEAD)
        scores = jax.nn.softmax(dot, axis=-1)
        out = jnp.einsum('bhst,bhtd->bhsd', scores, V)
        out = out.reshape(B, T_src, D_MODEL)
        return out @ Wh.T + bh

    def _L0_ffn_ref(x, norm_w, w1, w3, w2, gate_w, a1, b1, a3, b3, a2, b2):
        import jax, jax.numpy as jnp
        import numpy as np
        B, S, D, F, E, R, K = (1, 128, 256, 1024, 8, 16, 2)
        SCALING = 32.0 / 16.0
        EPS = 1e-06

        def _forward(x, norm_w, w1, w3, w2, gate_w, a1, b1, a3, b3, a2, b2):
            Bq, Sq, Dq = x.shape
            nx = x * jax.lax.rsqrt(jnp.mean(x * x, axis=-1, keepdims=True) + EPS) * norm_w
            t = nx.reshape(-1, Dq)
            probs = jax.nn.softmax(t @ gate_w.T, axis=-1)
            topw, topi = jax.lax.top_k(probs, K)
            topw = topw / jnp.sum(topw, axis=-1, keepdims=True)
            weights = jnp.sum(jax.nn.one_hot(topi, E, dtype=t.dtype) * topw[..., None], axis=1)
            base1 = t @ w1.T
            base3 = t @ w3.T
            h1 = base1[None] + SCALING * jnp.einsum('etr,efr->etf', jnp.einsum('td,erd->etr', t, a1), b1)
            h3 = base3[None] + SCALING * jnp.einsum('etr,efr->etf', jnp.einsum('td,erd->etr', t, a3), b3)
            act = jax.nn.silu(h1) * h3
            out_e = jnp.einsum('etf,df->etd', act, w2) + SCALING * jnp.einsum('etr,edr->etd', jnp.einsum('etf,erf->etr', act, a2), b2)
            out = jnp.einsum('te,etd->td', weights, out_e)
            return out.reshape(Bq, Sq, Dq)
        return _forward(x, norm_w, w1, w3, w2, gate_w, a1, b1, a3, b3, a2, b2)
    x = x + jnp.tanh(g_xattn[0]) * _L0_xattn_ref(_layernorm(x, axis=-1), ctx_1024, ctx_1024, L0_xattn_Wq, L0_xattn_bq, L0_xattn_Wk, L0_xattn_bk, L0_xattn_Wv, L0_xattn_bv, L0_xattn_Wh, L0_xattn_bh)
    x = x + jnp.tanh(g_ffn[0]) * _L0_ffn_ref(_layernorm(x, axis=-1), L0_ffn_norm_w, L0_ffn_w1, L0_ffn_w3, L0_ffn_w2, L0_ffn_gate_w, L0_ffn_a1, L0_ffn_b1, L0_ffn_a3, L0_ffn_b3, L0_ffn_a2, L0_ffn_b2)
    return x

_drawn_inputs = setup_inputs


def setup_inputs(seed=0):
    import zlib

    import numpy as np

    out = dict(_drawn_inputs(seed))
    spreads = {'L0_xattn_bq': (0.0, 0.494),
     'L0_xattn_bk': (0.0, 0.8),
     'L0_xattn_bv': (0.0, 0.1),
     'L0_xattn_bh': (0.0, 0.1),
     'L0_ffn_norm_w': (1.0, 0.6)}
    factors = {'L0_ffn_gate_w': 8.0,
     'L0_ffn_a1': 8.0,
     'L0_ffn_b1': 8.0,
     'L0_ffn_a3': 8.0,
     'L0_ffn_b3': 8.0,
     'L0_ffn_a2': 8.0,
     'L0_ffn_b2': 8.0}
    for name, (base, spread) in spreads.items():
        noise = np.random.default_rng([zlib.crc32(name.encode()), seed]).standard_normal(out[name].shape)
        drawn = base * np.exp(spread * noise) if base else spread * noise
        out[name] = jnp.asarray(drawn.astype(out[name].dtype))
    for name, factor in factors.items():
        out[name] = (out[name] * factor).astype(out[name].dtype)
    return out
```

```python
from contextlib import ExitStack

import concourse.bass as bass
from concourse import mybir

ALU = mybir.AluOpType
ACT = mybir.ActivationFunctionType
F32 = mybir.dt.float32
F32R = mybir.dt.float32r
U32 = mybir.dt.uint32
AX = mybir.AxisListType

B, S, D = 16, 100, 256
T, TP = 361, 362
H, DH = 16, 16
KT = D // 128
NQ = 4
T0 = [0, 121, 241]
TW = [121, 120, 120]
NT = len(T0)
UN = NQ * NT
VW = DH + 1
CS = 4 * S
NC = B // 4
E_, R, F = 8, 16, 1024
FT = F // 128
ER = E_ * R
LN_EPS, RMS_EPS = 1e-5, 1e-6


def spread(ap, axis, n):
    return ap.broadcast_to([n if i == axis else w for i, w in enumerate(ap.shape)])


def program(nc, x, ctxT, g_x, g_f, wqT, bq, wkT, bk, wvT, bv, whT, bh,
            norm_w, w1T, w3T, w2T, agT, b1T, b3T, a2T, b2T, out):
    es = ExitStack()
    with es:
        sb = lambda n, s, d=F32: es.enter_context(nc.sbuf_tensor(n, s, d))
        sem = lambda n: es.enter_context(nc.semaphore(n))
        o_dram = nc.dram_tensor("o_dram", [B, H * S, DH], F32, kind="Internal").ap()
        q_dram = nc.dram_tensor("q_dram", [2, D, B * S], F32, kind="Internal").ap()

        xs = sb("xs", [S, B, D])
        ident = sb("ident", [128, 128])
        stats = sb("stats", [S, B, 6])
        mv = sb("mv", [S, B, 2])
        rv = sb("rv", [S, B])
        rstd = sb("rstd", [S, B])
        nmr = sb("nmr", [S, B])
        gx = sb("gx", [128, 1])
        tgx = sb("tgx", [128, 1])
        nw = sb("nw", [128, KT])
        gf = sb("gf", [128, 1])
        tgf = sb("tgf", [128, 1])
        tmpv = sb("tmpv", [S, B])
        scl = sb("scl", [S, B])
        nms = sb("nms", [S, B])
        iota_e = sb("iota_e", [S, E_, R])

        with ExitStack() as early:
            sb0 = lambda n, s, d=F32: early.enter_context(nc.sbuf_tensor(n, s, d))
            wq = sb0("wq", [128, KT, D])
            xn = sb0("xn", [S, 2, D])
            xnT = sb0("xnT", [128, KT, B * S])
            qn = sb0("qn", [128, 2, KT, CS], F32R)
        w1 = sb("w1", [128, KT, F])
        w3 = sb("w3", [128, KT, F])
        b1s = sb("b1s", [ER, F])
        b3s = sb("b3s", [ER, F])
        w2 = sb("w2", [128, FT, D])
        a2 = sb("a2", [128, FT, ER])
        ag = sb("ag", [128, KT, E_ + 2 * ER])
        b2s = sb("b2s", [ER, D])

        mid = ExitStack()
        sba = lambda n, s, d=F32: mid.enter_context(nc.sbuf_tensor(n, s, d))
        wh = sba("wh", [128, KT, D])
        wst = sba("wst", [128, 2, KT, D])
        wkv = sba("wkv", [128, 2, 2, KT, D], F32R)
        bqs = sba("bqs", [128, KT])
        bks = sba("bks", [128, KT])
        bvs = sba("bvs", [S, D])
        bhs = sba("bhs", [S, D])
        tbh = sba("tbh", [S, D])
        craw = sba("craw", [128, KT, TP])
        cth = sba("cth", [128, 3, 2, KT, TP], F32R)
        kn = sba("kn", [128, 2, KT, TP], F32R)
        KS = [sba(f"KS{i}", [97, KT, 4, TP], F32R) for i in range(3)]
        QS = [sba(f"QS{i}", [97, KT * 4, 2, S], F32R) for i in range(3)]
        va = sba("va", [121, 3, NT, H, VW])
        pt = sba("pt", [121, 4, CS])
        nmax = sba("nmax", [S, H])
        crow = sba("crow", [H, S], F32R)
        osb = sba("osb", [128, NQ, S])
        rz = sba("rz", [S, H])
        on = sba("on", [S, H, DH])
        xr = sba("xr", [S, D])
        ot = sba("ot", [128, KT, S])
        mid.close()

        tx = sb("tx", [S, 2, D])
        tts = sb("tts", [128, 2, KT, S])
        ttT = sb("ttT", [128, KT, B * S])
        lgs = sb("lgs", [S, 2, E_])
        top = sb("top", [S, 2, 8])
        topi = sb("topi", [S, 2, 8], U32)
        topf = sb("topf", [S, 2, 2])
        dm = sb("dm", [S, 2])
        th = sb("th", [S, 2])
        wk2 = sb("wk2", [S, 2, 2])
        mask = sb("mask", [S, 2, 2, ER])
        um = sb("um", [S, 2, 2, 2, ER])
        u1 = sb("u1", [S, 2, 2, ER])
        utT = sb("utT", [ER, 2, 2, B * S])
        mkT = sb("mkT", [ER, 2, B * S])
        wbT = sb("wbT", [128, 2, B * S])
        sil = sb("sil", [128, 2, CS])
        hb = sb("hb", [128, 2, CS])
        aw = sb("aw", [128, 4, CS])
        aws = sb("aws", [128, FT, CS])
        zt = sb("zt", [ER, 2, CS])
        zm = sb("zm", [ER, CS])

        ps = [es.enter_context(nc.psum_tensor(f"bank{i}", [128, 512], F32)) for i in range(8)]
        pS, pT, pO, pP = ps[0:2], ps[2:4], ps[4], ps[5:8]
        pU, pZ, pX = ps[0:4], ps[4:6], ps[6:8]

        names = ("x_in w_in ctx_in cr xo xi on_b kout zero ident_ok st0 st1 st2 st3 rstd_ok nmr_ok xb_ok xn_ok xnT_t xnT_ok "
                 "q_mm q_h q_l q_out tg_ok tbh_ok wkv_h wkv_l ctx_h ctx_l pe_k act_kh dve_kl pe_v act_v "
                 "pe_cT act_c pe_s dve_s pe_st act_e pe_pv act_o pe_oT dve_rz dve_on pe_onT dve_ot pe_y dve_x1 done "
                 "fw_in iota_ok gf_in tgf_ok g0 g1 g2 g3 scl_ok nms_ok f_xn pe_t1 f_tt f_tta pe_gu f_max f_idx f_idf f_dm f_th f_w "
                 "f_mask f_um f_u1 f_d pe_t2 f_ut pe_t3 f_mw pe_a pe_b a_sil d_hb d_aw p_s pe_z d_zt d_zm pe_fy f_out").split()
        m = {n: sem("s_" + n) for n in names}
        KD, QD = 12 * 16, 6 * 16
        kst = [sem(f"s_kst{i}") for i in range(3)]
        qst = [sem(f"s_qst{i}") for i in range(3)]

        def stacked(per, b, buf):
            return per // 3 * b + (per - per // 3 * buf)

        block = es.enter_context(nc.Block())

        def wait(eng, name, value):
            s = m[name] if isinstance(name, str) else name
            if isinstance(value, int) and value <= 0:
                return
            eng.wait_ge(s, value)

        def pairs(eng, body):
            body(0)
            with eng.Fori(1, B // 2) as half:
                body(2 * half)

        def q_chunks(eng, body):
            body(0)
            with eng.Fori(1, NC) as c:
                body(c)

        def steps(eng, body):
            for i in (-2, -1, 0, 1):
                body(i, i % 3, i)
            with eng.Fori(0, 4) as turn:
                for k in range(2, 5):
                    body(3 * turn + k, k % 3, None)
            for i in (14, 15, 16, 17):
                body(i, i % 3, i)

        has_v = lambda p: p is None or 0 <= p + 1 < B
        has_k = lambda p: p is None or 0 <= p + 2 < B
        has_u = lambda p: p is None or 0 <= p < B
        has_o = lambda p: p is None or 0 <= p - 1 < B
        has_y = lambda p: p is None or 0 <= p - 2 < B

        def chunks(eng, body):
            body(0, True)
            with eng.Fori(1, NC - 1) as c:
                body(c, True)
            body(NC - 1, False)

        @block.sync
        def _(sp):
            sp.dma_start(xs[:], x.rearrange("b s d -> s b d")).then_inc(m["x_in"], 16)
            for dst, src in ((wq[:], wqT), (wh[:], whT), (wst[:, 0], wkT), (wst[:, 1], wvT)):
                sp.dma_start(dst, src).then_inc(m["w_in"], 16)
            for dst, src in ((bqs, bq), (bks, bk)):
                sp.dma_start(dst[:], src).then_inc(m["w_in"], 16)
            for dst, src in ((bhs, bh), (bvs, bv)):
                sp.dma_start(dst[:], spread(src.rearrange("(o d) -> o d", o=1), 0, S)).then_inc(m["w_in"], 16)
            sp.dma_start(gx[:], spread(g_x.rearrange("(o d) -> o d", o=1), 0, 128)).then_inc(m["w_in"], 16)
            sp.dma_start(gf[:], spread(g_f.rearrange("(o d) -> o d", o=1), 0, 128)).then_inc(m["gf_in"], 16)
            sp.dma_start(nw[:], norm_w).then_inc(m["gf_in"], 16)

            def ctx_load(b):
                wait(sp, "ctx_h", b)
                wait(sp, "ctx_l", b)
                sp.dma_start(craw[:, :, 0:T], ctxT[bass.ds(b, 1)].rearrange("o p k t -> p (o k) t")).then_inc(m["ctx_in"], 16)

            ctx_load(0)
            with sp.Fori(0, NC) as c:
                wait(sp, "q_l", c * KT + KT)
                for hl in range(2):
                    sp.dma_start(q_dram[hl].rearrange("(k p) t -> p k t", p=128)[:, :, bass.ds(c * CS, CS)],
                                 qn[:, hl].bitcast(F32)).then_inc(m["q_out"], 16)
            wait(sp, "q_out", 2 * NC * 16)

            def body(i, buf, p):
                nn = (buf + 2) % 3
                if has_k(p) and p != -2:
                    ctx_load(i + 2)
                if has_u(p):
                    wait(sp, "act_c", i + 1)
                    sp.dma_start(QS[buf][96:97, :, :, :].rearrange("o a b c -> o (a b c)").bitcast(F32),
                                 crow[:, :].bitcast(F32)).then_inc(m["cr"], 16)
                if has_o(p):
                    wait(sp, "on_b", i)
                    sp.dma_start(o_dram[bass.ds(i - 1, 1)].rearrange("o (h s) d -> s (o h) d", h=H),
                                 on[:]).then_inc(m["xo"], 16)
                if has_k(p):
                    wait(sp, "pe_st", i * UN)
                    for hl in range(2):
                        wait(sp, ("act_kh", "dve_kl")[hl], KT * (i + 3))
                        for g in range(4):
                            for row in ((0, 32), (64,))[hl]:
                                sp.dma_start(KS[nn][row:row + 32, :, g, :].bitcast(F32),
                                             kn[32 * g:32 * g + 32, hl, :, :].bitcast(F32)).then_inc(kst[nn], 16)
                if has_o(p):
                    wait(sp, "xo", 16 * i)
                    wait(sp, "pe_onT", i - 1)
                    sp.dma_start(xr[:], o_dram[bass.ds(i - 1, 1)].rearrange("o (r c) d -> (o r) (c d)", c=H)).then_inc(m["xi"], 16)

            for dst, src in ((w1, w1T), (w3, w3T), (b1s, b1T), (b3s, b3T), (w2, w2T), (a2, a2T), (ag, agT), (b2s, b2T)):
                sp.dma_start(dst[:], src).then_inc(m["fw_in"], 16)
            wait(sp, "zero", 4)
            steps(sp, body)
            with sp.Fori(0, B) as b:
                wait(sp, "f_out", b + 1)
                sp.dma_start(out[bass.ds(b, 1)].rearrange("o s d -> s (o d)"),
                             xs[:, bass.ds(b, 1), :].rearrange("s o d -> s (o d)")).then_inc(m["done"], 16)
            sp.wait_ge(m["done"], 16 * B)

        @block.gpsimd
        def _(pool):
            nc.gpsimd.memset(ident[:], 0.0).then_inc(m["ident_ok"], 1)
            pool.wait_ge(m["ident_ok"], 1)
            nc.gpsimd.affine_select(out=ident[:], in_=ident[:], compare_op=ALU.not_equal, fill=1.0, base=0,
                                    pattern=[[-1, 128]], channel_multiplier=1).then_inc(m["ident_ok"], 1)
            nc.gpsimd.iota(iota_e[:], pattern=[[1, E_], [0, R]], base=0, channel_multiplier=0,
                           allow_small_or_imprecise_dtypes=True).then_inc(m["iota_ok"], 1)

            def ctx_low(b, buf):
                wait(pool, "ctx_h", b + 1)
                nc.gpsimd.tensor_tensor(cth[:, buf, 1], craw[:], cth[:, buf, 0].bitcast(F32), ALU.subtract).then_inc(m["ctx_l"], 1)

            wait(pool, "xn_ok", B)
            wait(pool, "tbh_ok", 1)
            nc.gpsimd.tensor_tensor(xs[:], xs[:], spread(tbh[:, :].rearrange("p (o d) -> p o d", o=1), 1, B), ALU.add).then_inc(m["xb_ok"], 1)
            wait(pool, "zero", 4)
            wait(pool, "q_out", 2 * NC * 16)

            def body(i, buf, p):
                if has_o(p):
                    wait(pool, "dve_on", i)
                    o2 = on[:].rearrange("p h d -> p (h d)")
                    nc.gpsimd.tensor_tensor(o2, o2, bvs[:], ALU.add).then_inc(m["on_b"], 1)
                if has_k(p):
                    nn = (buf + 2) % 3
                    ctx_low(i + 2, nn)
                    wait(pool, "pe_st", i * UN)
                    for row, hl in ((0, 0), (32, 1), (64, 0)):
                        for odd in range(2):
                            src = q_dram[hl].rearrange("(n o d) t -> o d n t", o=2, d=DH)[odd]
                            pool.dma_start(QS[nn][row + DH * odd:row + DH * odd + DH, :, odd, :].bitcast(F32),
                                           src[:, :, bass.ds((i + 2) * S, S)]).then_inc(qst[nn], 16)

            steps(pool, body)

            def experts(c, more):
                for f in range(FT):
                    g = c * FT + f
                    wait(pool, "d_aw", 2 * g + 2)
                    if f == 0:
                        wait(pool, "pe_fy", 4 * c)
                    nc.gpsimd.tensor_tensor(aws[:, f], aw[:, 2 * (f % 2)], aw[:, 2 * (f % 2) + 1], ALU.add).then_inc(m["p_s"], 1)

            chunks(pool, experts)

        @block.scalar
        def _(act):
            act.wait_ge(m["w_in"], 9 * 16)
            nc.scalar.activation(tgx[:], gx[:], ACT.Tanh).then_inc(m["tg_ok"], 1)
            wait(act, "st3", 1)
            nc.scalar.activation(rstd[:], rv[:], ACT.Sqrt).then_inc(m["rstd_ok"], 1)
            def turned(b0):
                for k in range(2):
                    b = b0 + k
                    wait(act, "xnT_t", b + 1)
                    nc.scalar.activation(xnT[:, :, bass.ds(b * S, S)],
                                         pS[k][:, 0:KT * S].rearrange("p (k s) -> p k s", k=KT), ACT.Copy).then_inc(m["xnT_ok"], 1)

            pairs(act, turned)

            def q_high(c):
                for j in range(KT):
                    wait(act, "q_mm", c * KT + j + 1)
                    wait(act, "q_out", c * 32)
                    nc.scalar.activation(qn[:, 0, j], pT[j][:, 0:CS], ACT.Identity, bias=bqs[:, j:j + 1]).then_inc(m["q_h"], 1)

            q_chunks(act, q_high)

            def body(i, buf, p):
                if has_o(p):
                    wait(act, "pe_pv", i * UN)
                    wait(act, "pe_oT", i - 1)
                    nc.scalar.activation(osb[:].rearrange("p q s -> p (q s)"), pO[:, 0:CS], ACT.Copy).then_inc(m["act_o"], 1)
                if has_u(p):
                    wait(act, "pe_cT", i + 1)
                    wait(act, "cr", i * 16)
                    nc.scalar.activation(crow[:], pP[0][0:H, 0:S], ACT.Copy).then_inc(m["act_c"], 1)
                if has_v(p):
                    for t in range(NT):
                        b = i + 1
                        wait(act, "pe_v", NT * b + t + 1)
                        if t == 0:
                            wait(act, "pe_pv", i * UN)
                        nc.scalar.activation(va[0:TW[t], (buf + 1) % 3, t, :, 0:DH],
                                             pP[(1, 2, 1)[t]][0:TW[t], 0:D].rearrange("p (h d) -> p h d", h=H),
                                             ACT.Copy).then_inc(m["act_v"], 1)
                if has_k(p):
                    b = i + 2
                    for j in range(KT):
                        wait(act, "pe_k", KT * b + j + 1)
                        if j == 0:
                            if p is None or b > 0:
                                wait(act, kst[(buf + 1) % 3], stacked(KD, b - 1, (buf + 1) % 3))
                        nc.scalar.activation(kn[:, 0, j, :], pP[(2, 0)[j]][:, 0:TP], ACT.Identity,
                                             bias=bks[:, j:j + 1]).then_inc(m["act_kh"], 1)
                if has_u(p):
                    for u in range(UN):
                        n = i * UN + u
                        t = u % NT
                        wait(act, "pe_st", n + 1)
                        wait(act, "pe_pv", n - 3)
                        nc.scalar.activation(pt[0:TW[t], u % 4, :], pT[u % 2][0:TW[t], 0:CS], ACT.Exp,
                                             scale=float(DH) ** -0.5).then_inc(m["act_e"], 1)

            steps(act, body)

            wait(act, "g3", 1)
            nc.scalar.activation(scl[:], tmpv[:], ACT.Sqrt).then_inc(m["scl_ok"], 1)
            act.wait_ge(m["gf_in"], 32)
            nc.scalar.activation(tgf[:], gf[:], ACT.Tanh).then_inc(m["tgf_ok"], 1)

            def route_a(b, k):
                wait(act, "f_tt", b + 1)
                nc.scalar.activation(ttT[:, :, bass.ds(b * S, S)], tts[:, k % 2], ACT.Copy).then_inc(m["f_tta"], 1)

            def route_w(b, k):
                wait(act, "f_dm", b + 1)
                nc.scalar.activation(th[:, k % 2:k % 2 + 1], dm[:, k % 2:k % 2 + 1], ACT.Tanh, scale=0.5).then_inc(m["f_th"], 1)

            def route_b(b, k):
                wait(act, "pe_t2", b + 1)
                nc.scalar.activation(utT[:, :, :, bass.ds(b * S, S)].rearrange("p a b s -> p (a b) s"),
                                     pX[0][:, 0:4 * S].rearrange("p (n s) -> p n s", n=4), ACT.Copy, scale=2.0).then_inc(m["f_ut"], 1)
                wait(act, "pe_t3", b + 1)
                nc.scalar.activation(mkT[:, :, bass.ds(b * S, S)],
                                     pX[1][:, 0:2 * S].rearrange("p (n s) -> p n s", n=2), ACT.Copy, scale=2.0).then_inc(m["f_mw"], 1)
                nc.scalar.activation(wbT[:, :, bass.ds(b * S, S)],
                                     pX[1][:, 2 * S:4 * S].rearrange("p (n s) -> p n s", n=2), ACT.Copy).then_inc(m["f_mw"], 1)

            for k in range(4):
                route_a(k, k)
                route_w(k, k)
                route_b(k, k)

            def experts(c, more):
                for f in range(FT):
                    nb, k = 4 * (c + 1) + f // 2, f // 2
                    for slot in range(2):
                        if slot and more:
                            (route_a, route_b)[f % 2](nb, k)
                        n = 2 * (c * FT + f) + slot
                        wait(act, ("pe_a", "pe_b")[slot], c * FT + f + 1)
                        wait(act, "d_hb", n - 1 if f or slot else 2 * FT * c)
                        nc.scalar.activation(sil[:, slot], pU[2 * (f % 2)][:, 0:CS], ACT.Silu).then_inc(m["a_sil"], 1)
                    if more and f % 2 == 0:
                        route_w(nb, k)

            chunks(act, experts)

        @block.vector
        def _(dve):
            for i in range(3):
                nc.vector.memset(QS[i][:].bitcast(F32), 0.0).then_inc(m["zero"], 1)
                nc.vector.memset(KS[i][96:97].bitcast(F32), 1.0)
            nc.vector.memset(va[:, :, :, :, DH:VW], 1.0)
            nc.vector.memset(craw[:, :, T:TP], 0.0)
            nc.vector.memset(pO[:, :], 0.0).then_inc(m["zero"], 1)

            dve.wait_ge(m["x_in"], 16)
            with dve.Fori(0, B) as b:
                nc.vector.bn_stats(stats[:, bass.ds(b, 1), :].rearrange("p o s -> p (o s)"), xs[:, bass.ds(b, 1), :].rearrange("p o s -> p (o s)")).then_inc(m["st0"], 1)
            dve.wait_ge(m["st0"], B)
            for b in range(B):
                nc.vector.bn_aggr(mv[:, b, :], stats[:, b, :]).then_inc(m["st1"], 1)
            dve.wait_ge(m["st1"], B)
            nc.vector.tensor_scalar(rv[:], mv[:, :, 1], LN_EPS, None, ALU.add).then_inc(m["st2"], 1)
            dve.wait_ge(m["st2"], 1)
            nc.vector.reciprocal(rv[:], rv[:]).then_inc(m["st3"], 1)
            dve.wait_ge(m["rstd_ok"], 1)
            nc.vector.scalar_tensor_tensor(nmr[:], mv[:, :, 0], -1.0, rstd[:], ALU.mult, ALU.mult).then_inc(m["nmr_ok"], 1)
            dve.wait_ge(m["nmr_ok"], 1)
            def normed(b0):
                for k in range(2):
                    b = b0 + k
                    wait(dve, "xnT_t", b - 1)
                    nc.vector.tensor_scalar(xn[:, k, :], xs[:, bass.ds(b, 1), :].rearrange("p o s -> p (o s)"),
                                            rstd[:, bass.ds(b, 1)], nmr[:, bass.ds(b, 1)], ALU.mult, ALU.add).then_inc(m["xn_ok"], 1)

            pairs(dve, normed)
            dve.wait_ge(m["w_in"], 9 * 16)
            dve.wait_ge(m["tg_ok"], 1)
            nc.vector.tensor_scalar(tbh[:], bhs[:], tgx[0:S, :], None, ALU.mult).then_inc(m["tbh_ok"], 1)
            for w in range(2):
                nc.vector.tensor_copy(wkv[:, w, 0], wst[:, w]).then_inc(m["wkv_h"], 1)
            dve.wait_ge(m["wkv_h"], 2)
            for w in range(2):
                nc.vector.tensor_tensor(wkv[:, w, 1], wst[:, w], wkv[:, w, 0].bitcast(F32), ALU.subtract).then_inc(m["wkv_l"], 1)

            def ctx_high(b, buf):
                wait(dve, "ctx_in", 16 * (b + 1))
                wait(dve, "pe_v", NT * (b - 2))
                nc.vector.tensor_copy(cth[:, buf, 0], craw[:]).then_inc(m["ctx_h"], 1)

            def q_low(c):
                for j in range(KT):
                    wait(dve, "q_h", c * KT + j + 1)
                    nc.vector.scalar_tensor_tensor(qn[:, 1, j], pT[j][:, 0:CS], bqs[:, j:j + 1], qn[:, 0, j].bitcast(F32),
                                                   ALU.add, ALU.subtract).then_inc(m["q_l"], 1)

            q_chunks(dve, q_low)

            def body(i, buf, p):
                if has_k(p):
                    ctx_high(i + 2, (buf + 2) % 3)
                if has_o(p):
                    wait(dve, "pe_oT", i)
                    o3 = pP[0][0:S, :].rearrange("p (h c) -> p h c", c=32)
                    nc.vector.reciprocal(rz[:].rearrange("p (h o) -> p h o", o=1), o3[:, :, DH:VW]).then_inc(m["dve_rz"], 1)
                    wait(dve, "dve_rz", i)
                    wait(dve, "xo", 16 * (i - 1))
                    nc.vector.tensor_tensor(on[:], o3[:, :, 0:DH], spread(rz[:].rearrange("p (h o) -> p h o", o=1), 2, DH),
                                            ALU.mult).then_inc(m["dve_on"], 1)
                if has_k(p):
                    b = i + 2
                    for j in range(KT):
                        wait(dve, "act_kh", KT * b + j + 1)
                        nc.vector.scalar_tensor_tensor(kn[:, 1, j, :], pP[(2, 0)[j]][:, 0:TP], bks[:, j:j + 1],
                                                       kn[:, 0, j, :].bitcast(F32), ALU.add, ALU.subtract).then_inc(m["dve_kl"], 1)

                def head(h):
                    n = (i + 1) * H + h
                    wait(dve, "pe_s", n + 1)
                    if h == 0:
                        wait(dve, "pe_cT", i + 1)
                    nc.vector.tensor_reduce(nmax[:, h:h + 1], pS[h % 2][0:S, 0:T], AX.X, ALU.max, negate=True).then_inc(m["dve_s"], 1)

                if has_v(p):
                    for h in range(4):
                        head(h)
                if has_y(p):
                    wait(dve, "pe_onT", i - 1)
                    nc.vector.tensor_copy(ot[:].rearrange("p k s -> p (k s)"), pP[1][:, 0:KT * S]).then_inc(m["dve_ot"], 1)
                if has_v(p):
                    for h in range(4, 8):
                        head(h)
                if has_y(p):
                    wait(dve, "pe_y", i - 1)
                    if p is None:
                        wait(dve, "xb_ok", 1)
                    xb = xs[:, bass.ds(i - 2, 1), :].rearrange("p o s -> p (o s)")
                    nc.vector.scalar_tensor_tensor(xb, pP[2][0:S, 0:D], tgx[0:S, :], xb, ALU.mult, ALU.add).then_inc(m["dve_x1"], 1)
                if has_v(p):
                    for h in range(8, H):
                        head(h)

            steps(dve, body)

            dve.wait_ge(m["dve_x1"], B)
            with dve.Fori(0, B) as b:
                nc.vector.bn_stats(stats[:, bass.ds(b, 1), :].rearrange("p o s -> p (o s)"),
                                   xs[:, bass.ds(b, 1), :].rearrange("p o s -> p (o s)")).then_inc(m["g0"], 1)
            dve.wait_ge(m["g0"], B)
            for b in range(B):
                nc.vector.bn_aggr(mv[:, b, :], stats[:, b, :]).then_inc(m["g1"], 1)
            dve.wait_ge(m["g1"], B)
            nc.vector.tensor_scalar(tmpv[:], mv[:, :, 1], 1.0 + RMS_EPS, RMS_EPS * LN_EPS, ALU.mult, ALU.add).then_inc(m["g2"], 1)
            dve.wait_ge(m["g2"], 1)
            nc.vector.reciprocal(tmpv[:], tmpv[:]).then_inc(m["g3"], 1)
            dve.wait_ge(m["scl_ok"], 1)
            nc.vector.scalar_tensor_tensor(nms[:], mv[:, :, 0], -1.0, scl[:], ALU.mult, ALU.mult).then_inc(m["nms_ok"], 1)
            dve.wait_ge(m["nms_ok"], 1)
            dve.wait_ge(m["iota_ok"], 1)
            dve.wait_ge(m["tgf_ok"], 1)

            def route_x(b, k):
                kb = k % 2
                wait(dve, "pe_t1", b - 1)
                nc.vector.tensor_scalar(tx[:, kb, :], xs[:, bass.ds(b, 1), :].rearrange("p o s -> p (o s)"),
                                        scl[:, bass.ds(b, 1)], nms[:, bass.ds(b, 1)], ALU.mult, ALU.add).then_inc(m["f_xn"], 1)

            def route_a(b, k):
                kb = k % 2
                wait(dve, "pe_t1", b + 1)
                wait(dve, "pe_gu", b - 1)
                wait(dve, "f_tta", b - 1)
                nc.vector.tensor_tensor(tts[:, kb], pX[0][:, 0:KT * S].rearrange("p (k s) -> p k s", k=KT),
                                        spread(nw[:].rearrange("p (k o) -> p k o", o=1), 2, S), ALU.mult).then_inc(m["f_tt"], 1)

            def route_b(b, k):
                kb = k % 2
                lg = pX[1][0:S, 0:E_]
                uu = pX[1][0:S, E_:E_ + 2 * ER].rearrange("p (a e) -> p a e", a=2)
                wait(dve, "pe_gu", b + 1)
                nc.vector.tensor_copy(lgs[:, kb], lg)
                nc.vector.max(top[:, kb], lg).then_inc(m["f_max"], 1)
                wait(dve, "f_th", b - 1)
                wait(dve, "f_max", b + 1)
                nc.vector.tensor_tensor(dm[:, kb:kb + 1], top[:, kb, 0:1], top[:, kb, 1:2], ALU.subtract).then_inc(m["f_dm"], 1)
                nc.vector.max_index(topi[:, kb], top[:, kb], lg).then_inc(m["f_idx"], 1)
                wait(dve, "f_idx", b + 1)
                nc.vector.tensor_copy(topf[:, kb], topi[:, kb, 0:2]).then_inc(m["f_idf"], 1)
                wait(dve, "f_idf", b + 1)
                wait(dve, "pe_t3", b - 1)
                for slot in range(2):
                    nc.vector.tensor_scalar(mask[:, kb, slot], iota_e[:].rearrange("p e r -> p (e r)"),
                                            topf[:, kb, slot:slot + 1], None, ALU.is_equal).then_inc(m["f_mask"], 1)
                wait(dve, "f_mask", 2 * b + 2)
                mk = lambda slot: spread(mask[:, kb, slot:slot + 1, :], 1, 2)
                wait(dve, "pe_t2", b - 1)
                nc.vector.tensor_tensor(um[:, kb, 0], uu, mk(0), ALU.mult).then_inc(m["f_um"], 1)
                nc.vector.tensor_tensor(u1[:, kb], uu, mk(1), ALU.mult).then_inc(m["f_u1"], 1)
                wait(dve, "f_um", b + 1)
                wait(dve, "f_u1", b + 1)
                nc.vector.tensor_tensor(um[:, kb, 1], u1[:, kb], um[:, kb, 0], ALU.subtract).then_inc(m["f_d"], 1)
                wait(dve, "f_th", b + 1)
                for slot, half in ((0, 0.5), (1, -0.5)):
                    nc.vector.tensor_scalar(wk2[:, kb, slot:slot + 1], th[:, kb:kb + 1], half, 0.5, ALU.mult, ALU.add).then_inc(m["f_w"], 1)

            for k in range(4):
                route_x(k, k)
                route_a(k, k)
                route_b(k, k)

            def experts(c, more):
                cols = bass.ds(c * CS, CS)
                for f in range(FT):
                    nb, k = 4 * (c + 1) + f // 2, f // 2
                    if more and f % 2 == 0:
                        route_x(nb, k)
                    for slot in range(2):
                        if slot and more and f % 2 == 0:
                            route_a(nb, k)
                        g = c * FT + f
                        n = 2 * g + slot
                        wait(dve, "a_sil", n + 1)
                        if slot == 0 and f == 0:
                            wait(dve, "f_mw", 8 * (c + 1))
                        nc.vector.tensor_tensor(hb[:, slot], sil[:, slot], pU[2 * (f % 2) + 1][:, 0:CS], ALU.mult).then_inc(m["d_hb"], 1)
                        wait(dve, "d_hb", n + 1)
                        if f >= 2:
                            wait(dve, "pe_z", g - 1)
                            wait(dve, "p_s", g - 1)
                        nc.vector.tensor_tensor(aw[:, 2 * (f % 2) + slot], hb[:, slot],
                                                wbT[:, slot, cols], ALU.mult).then_inc(m["d_aw"], 1)
                    if more and f % 2 == 0:
                        route_b(nb, k)
                wait(dve, "pe_z", FT * (c + 1))
                for slot in range(2):
                    nc.vector.tensor_tensor(zt[:, slot], pZ[slot][:, 0:CS], mkT[:, slot, cols], ALU.mult).then_inc(m["d_zt"], 1)
                wait(dve, "d_zt", 2 * c + 2)
                wait(dve, "pe_fy", 4 * c)
                nc.vector.tensor_tensor(zm[:], zt[:, 0], zt[:, 1], ALU.add).then_inc(m["d_zm"], 1)
                for k in range(4):
                    b = 4 * c + k
                    wait(dve, "pe_fy", b + 1)
                    xb = xs[:, bass.ds(b, 1), :].rearrange("p o s -> p (o s)")
                    nc.vector.scalar_tensor_tensor(xb, pX[k % 2][0:S, 0:D], tgf[0:S, :], xb, ALU.mult, ALU.add).then_inc(m["f_out"], 1)

            chunks(dve, experts)

        @block.tensor
        def _(pe):
            mm = nc.tensor.matmul
            pe.wait_ge(m["ident_ok"], 2)
            def turn(b0):
                for k in range(2):
                    wait(pe, "xn_ok", b0 + k + 1)
                    wait(pe, "xnT_ok", b0 + k - 1)
                    for j in range(KT):
                        last = nc.tensor.transpose(pS[k][:, j * S:(j + 1) * S], xn[:, k, j * 128:(j + 1) * 128], ident[0:S, 0:S])
                    last.then_inc(m["xnT_t"], 1)

            pairs(pe, turn)
            pe.wait_ge(m["xnT_ok"], B)
            pe.wait_ge(m["w_in"], 9 * 16)
            def q_proj(c):
                for j in range(KT):
                    wait(pe, "q_l", (c - 1) * KT + j + 1)
                    for k in range(KT):
                        last = mm(pT[j][:, 0:CS], wq[:, k, j * 128:(j + 1) * 128], xnT[:, k, bass.ds(c * CS, CS)],
                                  start=k == 0, stop=k == KT - 1)
                    last.then_inc(m["q_mm"], 1)

            q_chunks(pe, q_proj)
            pe.wait_ge(m["wkv_l"], 2)
            pe.wait_ge(m["zero"], 4)

            TERMS = ((0, 0), (0, 1), (1, 0))

            def body(i, buf, p):
                nxt, nn = (buf + 1) % 3, (buf + 2) % 3

                def k_proj(j):
                    b = i + 2
                    if j == 0:
                        wait(pe, "ctx_l", b + 1)
                    n = 0
                    for k in range(KT):
                        for hw, hc in TERMS:
                            last = mm(pP[(2, 0)[j]][:, 0:TP], wkv[:, 0, hw, k, j * 128:(j + 1) * 128],
                                      cth[:, nn, hc, k, :], start=n == 0, stop=n == 5)
                            n += 1
                    last.then_inc(m["pe_k"], 1)

                def v_proj(t):
                    n = 0
                    for k in range(KT):
                        for hw, hc in TERMS:
                            last = mm(pP[(1, 2, 1)[t]][0:TW[t], 0:D], cth[:, nxt, hc, k, T0[t]:T0[t] + TW[t]],
                                      wkv[:, 1, hw, k, :], start=n == 0, stop=n == 5)
                            n += 1
                    last.then_inc(m["pe_v"], 1)

                def o_transpose():
                    wait(pe, "act_o", i)
                    if has_u(p):
                        wait(pe, "act_c", i + 1)
                    else:
                        wait(pe, "dve_on", i - 1)
                    for q in range(NQ):
                        last = nc.tensor.transpose(pP[0][0:S, q * 128:(q + 1) * 128], osb[:, q, :], ident[:])
                    last.then_inc(m["pe_oT"], 1)

                def on_transpose():
                    wait(pe, "xi", 16 * (i - 1))
                    if has_v(p):
                        wait(pe, "act_v", NT * (i + 2))
                    for j in range(KT):
                        last = nc.tensor.transpose(pP[1][:, j * S:(j + 1) * S],
                                                   xr[:, j * 128:(j + 1) * 128], ident[0:S, 0:S])
                    last.then_inc(m["pe_onT"], 1)

                def y_proj():
                    wait(pe, "dve_ot", i - 1)
                    if has_k(p):
                        wait(pe, "dve_kl", KT * (i + 2) + 1)
                    else:
                        wait(pe, "dve_x1", i - 2)
                    for k in range(KT):
                        last = mm(pP[2][0:S, 0:D], ot[:, k, :], wh[:, k, :], start=k == 0, stop=k == KT - 1)
                    last.then_inc(m["pe_y"], 1)

                def s_head(h):
                    n = (i + 1) * H + h
                    if h == 0:
                        wait(pe, kst[nxt], stacked(KD, i + 1, nxt))
                    if h == 0:
                        wait(pe, qst[nxt], stacked(QD, i + 1, nxt))
                    wait(pe, "dve_s", n - 1)
                    pr = h // 2
                    mm(pS[h % 2][0:S, 0:TP], QS[nxt][0:96, pr, h % 2, :], KS[nxt][0:96, pr // 4, pr % 4, :],
                       start=True, stop=True).then_inc(m["pe_s"], 1)

                def st_unit(u):
                    n = i * UN + u
                    q, t = u // NT, u % NT
                    if u == 0:
                        wait(pe, "cr", 16 * (i + 1))
                    wait(pe, "act_e", n - 1)
                    for pr in (2 * q, 2 * q + 1):
                        last = mm(pT[u % 2][0:TW[t], (pr % 2) * 2 * S:(pr % 2 + 1) * 2 * S],
                                  KS[buf][:, pr // 4, pr % 4, T0[t]:T0[t] + TW[t]],
                                  QS[buf][:, pr].rearrange("p o s -> p (o s)"), start=True, stop=True)
                    last.then_inc(m["pe_st"], 1)

                def pv_unit(u):
                    n = i * UN + u
                    q, t = u // NT, u % NT
                    if u == 0:
                        wait(pe, "act_o", i)
                        wait(pe, "act_v", NT * (i + 1))
                    wait(pe, "act_e", n + 1)
                    for g in range(4):
                        last = mm(pO[32 * g:32 * g + VW, q * S:(q + 1) * S], va[0:TW[t], buf, t, 4 * q + g, :],
                                  pt[0:TW[t], u % 4, g * S:(g + 1) * S], start=t == 0, stop=t == NT - 1)
                    last.then_inc(m["pe_pv"], 1)

                if has_u(p):
                    wait(pe, "dve_s", H * (i + 1))
                    if p is None or p < B - 1:
                        wait(pe, "dve_kl", KT * (i + 2))
                    else:
                        wait(pe, "dve_on", i - 1)
                    nc.tensor.transpose(pP[0][0:H, 0:S], nmax[:], ident[0:S, 0:S]).then_inc(m["pe_cT"], 1)
                if has_v(p):
                    wait(pe, "act_v", NT * (i + 1))
                    v_proj(0)
                    if p == -1:
                        wait(pe, "dve_kl", 1)
                    v_proj(1)
                if has_o(p):
                    o_transpose()
                if has_v(p):
                    wait(pe, "act_v", NT * (i + 1) + 1)
                    v_proj(2)
                if has_k(p):
                    if p is None or p + 1 >= 0:
                        wait(pe, "act_v", NT * (i + 1) + 2)
                    k_proj(0)
                    if p == -1:
                        wait(pe, "dve_kl", 2)
                    if p == 0:
                        wait(pe, "act_c", 1)
                    if has_o(p):
                        wait(pe, "dve_on", i)
                    k_proj(1)
                if not has_u(p):
                    if has_v(p):
                        for h in range(H):
                            s_head(h)
                    if has_y(p):
                        on_transpose()
                        y_proj()
                    return
                st_unit(0)
                if has_v(p):
                    s_head(0)
                    s_head(1)
                st_unit(1)
                if has_y(p):
                    on_transpose()
                for u in range(2, UN + 2):
                    if u < UN:
                        st_unit(u)
                    if has_v(p):
                        a = min(H, 2 + (u - 2) * 3 // 2)
                        for h in range(a, min(H, 2 + (u - 1) * 3 // 2)):
                            s_head(h)
                    pv_unit(u - 2)
                    if u == 4 and has_y(p):
                        y_proj()

            steps(pe, body)
            pe.wait_ge(m["fw_in"], 8 * 16)

            def route_1(b, k):
                wait(pe, "f_xn", b + 1)
                wait(pe, "f_ut", b)
                for j in range(KT):
                    last = nc.tensor.transpose(pX[0][:, j * S:(j + 1) * S], tx[:, k % 2, j * 128:(j + 1) * 128], ident[0:S, 0:S])
                last.then_inc(m["pe_t1"], 1)

            def route_2(b, k):
                wait(pe, "f_tt", b + 1)
                wait(pe, "f_mw", 2 * b)
                for j in range(KT):
                    last = mm(pX[1][0:S, 0:E_ + 2 * ER], tts[:, k % 2, j, :], ag[:, j, :], start=j == 0, stop=j == KT - 1)
                last.then_inc(m["pe_gu"], 1)

            def route_3(b, k):
                wait(pe, "f_d", b + 1)
                for a in range(2):
                    for n in range(2):
                        q = 2 * a + n
                        last = nc.tensor.transpose(pX[0][:, q * S:(q + 1) * S], um[:, k % 2, a, n, :], ident[0:S, 0:S])
                last.then_inc(m["pe_t2"], 1)
                wait(pe, "f_w", 2 * b + 2)
                for slot in range(2):
                    nc.tensor.transpose(pX[1][:, slot * S:(slot + 1) * S], mask[:, k % 2, slot, :], ident[0:S, 0:S])
                for slot in range(2):
                    last = nc.tensor.transpose(pX[1][:, (2 + slot) * S:(3 + slot) * S],
                                               spread(wk2[:, k % 2, slot:slot + 1], 1, 128), ident[0:S, 0:S])
                last.then_inc(m["pe_t3"], 1)

            for k in range(4):
                route_1(k, k)
                route_2(k, k)
                route_3(k, k)

            def experts(c, more):
                cols = bass.ds(c * CS, CS)

                def up(f, slot):
                    g = c * FT + f
                    if slot == 0:
                        if f >= 2:
                            wait(pe, "d_hb", 2 * g - 2)
                        else:
                            wait(pe, "d_hb", 2 * FT * c)
                    else:
                        wait(pe, "d_hb", 2 * g + 1)
                    fs = slice(f * 128, (f + 1) * 128)
                    for a, (w, bb) in enumerate(((w1, b1s), (w3, b3s))):
                        bank = pU[2 * (f % 2) + a][:, 0:CS]
                        if slot == 0:
                            for j in range(KT):
                                mm(bank, w[:, j, fs], ttT[:, j, cols], start=j == 0, stop=False)
                        last = mm(bank, bb[:, fs], utT[:, slot, a, cols], start=False, stop=True, skip_group_check=slot == 1)
                    last.then_inc(m[("pe_a", "pe_b")[slot]], 1)

                def down_low(f):
                    g = c * FT + f
                    wait(pe, "d_aw", 2 * g + 2)
                    if f == 0:
                        wait(pe, "d_zm", c)
                    for slot in range(2):
                        last = mm(pZ[slot][:, 0:CS], a2[:, f, :], aw[:, 2 * (f % 2) + slot, :], start=f == 0, stop=f == FT - 1)
                    last.then_inc(m["pe_z"], 1)

                wait(pe, "f_ut", 4 * (c + 1))
                wait(pe, "f_tta", 4 * (c + 1))
                wait(pe, "f_out", 4 * c)
                up(0, 0)
                for f in range(FT):
                    if more and f % 2 == 0:
                        route_1(4 * (c + 1) + f // 2, f // 2)
                    if f + 1 < FT:
                        up(f + 1, 0)
                    if more:
                        (route_2, route_3)[f % 2](4 * (c + 1) + f // 2, f // 2)
                    up(f, 1)
                    if f >= 1:
                        down_low(f - 1)
                down_low(FT - 1)
                wait(pe, "p_s", FT * (c + 1))
                wait(pe, "d_zm", c + 1)
                if more:
                    wait(pe, "f_ut", 4 * (c + 2))
                    wait(pe, "f_mw", 8 * (c + 2))
                for k in range(4):
                    if k >= 2:
                        wait(pe, "f_out", 4 * c + k - 1)
                    ks = slice(k * S, (k + 1) * S)
                    for f in range(FT):
                        mm(pX[k % 2][0:S, 0:D], aws[:, f, ks], w2[:, f, :], start=f == 0, stop=False)
                    mm(pX[k % 2][0:S, 0:D], zm[:, ks], b2s[:], start=False, stop=True).then_inc(m["pe_fy"], 1)

            chunks(pe, experts)


INPUTS = ("x ctxT g_x g_f wqT bq wkT bk wvT bv whT bh norm_w w1T w3T w2T agT b1T b3T a2T b2T").split()


def kernel(**inputs):
    import numpy as np
    import concourse.bacc as bacc
    from concourse.bass_utils import run_bass_kernel_spmd

    a = {k: np.asarray(v) for k, v in inputs.items()}
    halves = lambda w: np.ascontiguousarray(w.T.reshape(w.shape[1] // 128, 128, w.shape[0]).transpose(1, 0, 2))
    cols = lambda v: np.ascontiguousarray(v.reshape(-1, 128).T)
    p = lambda n: a["L0_xattn_" + n]
    f = lambda n: a["L0_ffn_" + n]
    gate_a = np.concatenate([f("gate_w"), f("a1").reshape(ER, D), f("a3").reshape(ER, D)], axis=0)
    laid = {
        "x": a["x"],
        "ctxT": np.ascontiguousarray(a["ctx_1024"].transpose(0, 2, 1).reshape(B, KT, 128, T).transpose(0, 2, 1, 3)),
        "g_x": a["g_xattn"], "g_f": a["g_ffn"],
        "wqT": halves(p("Wq")), "bq": cols(p("bq")), "wkT": halves(p("Wk")), "bk": cols(p("bk")),
        "wvT": halves(p("Wv")), "bv": p("bv"), "whT": halves(p("Wh")), "bh": p("bh"),
        "norm_w": cols(f("norm_w")), "w1T": halves(f("w1")), "w3T": halves(f("w3")), "w2T": halves(f("w2")),
        "agT": halves(gate_a),
        "b1T": np.ascontiguousarray(f("b1").transpose(0, 2, 1).reshape(ER, F)),
        "b3T": np.ascontiguousarray(f("b3").transpose(0, 2, 1).reshape(ER, F)),
        "a2T": halves(f("a2").reshape(ER, F)),
        "b2T": np.ascontiguousarray(f("b2").transpose(0, 2, 1).reshape(ER, D)),
    }
    nc = bacc.Bacc("TRN2", target_bir_lowering=False, num_devices=1)
    arrays, args = {}, []
    for n in INPUTS:
        arrays[n] = laid[n]
        args.append(nc.dram_tensor(n, laid[n].shape, mybir.dt.from_np(laid[n].dtype), kind="ExternalInput").ap())
    args.append(nc.dram_tensor("y", (B, S, D), F32, kind="ExternalOutput").ap())
    program(nc, *args)
    r = run_bass_kernel_spmd(nc, [arrays], core_ids=[0])
    return r.results[0]["y"]
```
